# Optimizing a Trainium2 kernel written in Bass

```python
import numpy as np
import jax
import jax.numpy as jnp

def _softmax(x, axis=-1):
    return jax.nn.softmax(x, axis=axis)

def _gelu(x):
    return jax.nn.gelu(x, approximate=True)

def _silu(x):
    return jax.nn.silu(x)

def _sigmoid(x):
    return jax.nn.sigmoid(x)

def _layernorm(x, axis=-1, eps=1e-05):
    m = jnp.mean(x, axis=axis, keepdims=True)
    v = jnp.var(x, axis=axis, keepdims=True)
    return (x - m) / jnp.sqrt(v + eps)

def _scatter_add(tgt, idx, src, axis=0):
    return tgt.at[idx].add(src)

def _segment_sum(src, seg, n):
    return jax.ops.segment_sum(src, seg, n)
kernel_name = 'mk_cond_resid_d1_seqx_r4_7cbe75'

def setup_inputs(seed: int=0):
    np.random.seed(seed)
    _w = jnp.asarray

    def _rec_inputs():
        import jax
        import jax.numpy as jnp
        _rk = jax.random.key(seed)
        x = 7.22e-05 + 1 * jax.random.normal(jax.random.fold_in(_rk, 1), (32, 256, 256), jnp.float32)
        _lenS = 256 - jax.random.randint(jax.random.fold_in(_rk, 7), (32,), 0, max(1, 256 // 4) + 1, jnp.int32)
        _lenS2 = 256 - jax.random.randint(jax.random.fold_in(_rk, 8), (32,), 0, max(1, 256 // 4) + 1, jnp.int32)
        cond_8 = jax.random.uniform(jax.random.fold_in(_rk, 11), (32, 8), jnp.float32, 0.0, 0.999837)
        return (x, cond_8)
    x, cond_8 = _rec_inputs()

    def _L0_cond_setup():
        import jax, jax.numpy as jnp
        import numpy as np
        key = jax.random.key(seed)
        k1, k2, k3, k4, k5 = jax.random.split(key, 5)
        B, N, T, O, G = (32, 64, 256, 256, 8)
        x = jax.random.normal(k1, (B, N, T), dtype=jnp.float32)
        y = jax.random.uniform(k2, (B, G), dtype=jnp.float32)
        weight = jax.random.normal(k3, (G, O, T), dtype=jnp.float32) * (1.0 / np.sqrt(T))
        mask = jax.random.uniform(k4, (O, T), dtype=jnp.float32)
        bias = jax.random.normal(k5, (O,), dtype=jnp.float32)
        return {'x': x, 'y': y, 'weight': weight, 'mask': mask, 'bias': bias}
    _L0_cond_all = _L0_cond_setup()
    _L0_cond_in = {k: v for k, v in _L0_cond_all.items() if k in ('weight', 'mask', 'bias')}
    del _L0_cond_all
    return {'x': x, 'cond_8': cond_8, 'L0_cond_weight': _L0_cond_in['weight'], 'L0_cond_mask': _L0_cond_in['mask'], 'L0_cond_bias': _L0_cond_in['bias']}

def reference(x, cond_8, L0_cond_weight, L0_cond_mask, L0_cond_bias):
    import jax
    import jax.numpy as jnp

    def _L0_cond_ref(x, y, weight, mask, bias):
        import jax, jax.numpy as jnp
        import numpy as np
        masked_w = weight * mask[None, :, :]
        w_bot = jnp.einsum('bg,got->bot', y, masked_w)
        return jnp.einsum('bnt,bot->bno', x, w_bot) + bias
    x = x + _L0_cond_ref(x, cond_8, L0_cond_weight, L0_cond_mask, L0_cond_bias)
    return x

_drawn_inputs = setup_inputs


def setup_inputs(seed=0):
    import zlib

    import numpy as np

    out = dict(_drawn_inputs(seed))
    spreads = {}
    factors = {}
    for name, (base, spread) in spreads.items():
        noise = np.random.default_rng([zlib.crc32(name.encode()), seed]).standard_normal(out[name].shape)
        drawn = base * np.exp(spread * noise) if base else spread * noise
        out[name] = jnp.asarray(drawn.astype(out[name].dtype))
    for name, factor in factors.items():
        out[name] = (out[name] * factor).astype(out[name].dtype)
    return out
```

```python
from contextlib import ExitStack

import concourse.bass as bass
from concourse import mybir

P = 128
F32 = mybir.dt.float32
F32R = mybir.dt.float32r
ALU = mybir.AluOpType
ACT = mybir.ActivationFunctionType
AX_X = mybir.AxisListType.X

BANK = 512
XS = 4
CH = 2


def conditional_residual(nc, x, cond, weight, mask, bias, out):
    B, N, T = x.shape
    G, O, _ = weight.shape
    R = P // G
    Q = O // R
    KC = T // P
    J = N // P
    PAIRS = B // 2
    CHUNKS = Q // CH
    GEN = CHUNKS * KC
    LOADS = 16 * (1 + G) * (CHUNKS // XS)
    PAIR = 2 * J * T
    assert O == N == T and B * R == BANK and CH * BANK == PAIR == KC * BANK and J * O == BANK
    assert PAIRS % XS == 0 and CHUNKS % XS == 0

    x_dram = x.rearrange("(i b) (p j) t -> i p b (j t)", b=2, j=J)
    out_dram = out.rearrange("(i b) (p j) o -> i p b (j o)", b=2, j=J)
    weight_dram = weight.rearrange("g (r q) t -> (g r) (q t)", q=Q)
    mask_dram = mask.rearrange("(r q) t -> r (q t)", q=Q)

    with ExitStack() as ctx:
        def sb(name, shape, dt=F32):
            return ctx.enter_context(nc.sbuf_tensor(name, shape, dt))

        def psum(name, shape):
            return ctx.enter_context(nc.psum_tensor(name, shape, F32))

        def sem(name):
            return ctx.enter_context(nc.semaphore(name))

        w_hi = sb("w_hi", [P, KC, B, Q, R], F32R)
        w_lo = sb("w_lo", [P, KC, B, Q, R], F32R)
        mw_hi = sb("mw_hi", [P, 2, CH, T], F32R)
        mw_lo = sb("mw_lo", [P, 2, CH, T], F32R)
        y_hi = sb("y_hi", [P, B, R], F32R)
        y_lo = sb("y_lo", [P, B, R], F32R)
        x_ring = sb("x_ring", [P, XS, PAIR])
        out_ring = sb("out_ring", [P, XS, PAIR])
        xt_hi = sb("xt_hi", [P, XS, KC, 2, J, P], F32R)
        xt_lo = sb("xt_lo", [P, XS, KC, 2, J, P], F32R)
        bias_rows = sb("bias_rows", [P, O])
        ident = sb("ident", [P, P])
        cond_rows = sb("cond_rows", [B, G])
        cond_wide = sb("cond_wide", [B, G, R])
        diag = sb("diag", [P, R])
        yt_hi = sb("yt_hi", [P, B], F32R)
        yt_lo = sb("yt_lo", [P, B])

        transposes = psum("transposes", [P, 2, PAIR])
        products = psum("products", [P, 2, PAIR])

        cond_loaded = sem("cond_loaded")
        bias_loaded = sem("bias_loaded")
        ident_zeroed = sem("ident_zeroed")
        ident_ready = sem("ident_ready")
        cond_widened = sem("cond_widened")
        yt_ready = sem("yt_ready")
        yt_hi_ready = sem("yt_hi_ready")
        y_parts_ready = sem("y_parts_ready")
        y_ready = sem("y_ready")
        slot_moved = [sem(f"slot_moved{s}") for s in range(XS)]
        masked = sem("masked")
        mw_hi_ready = sem("mw_hi_ready")
        mw_lo_ready = sem("mw_lo_ready")
        x_loaded = [sem(f"x_loaded{s}") for s in range(XS)]
        transposed = sem("transposed")
        xt_hi_ready = sem("xt_hi_ready")
        xt_lo_ready = sem("xt_lo_ready")
        x_biased = sem("x_biased")
        products_ready = sem("products_ready")
        w_hi_ready = sem("w_hi_ready")
        evacuated = sem("evacuated")

        block = ctx.enter_context(nc.Block())

        def stage(slot):
            whole = out_ring[:, slot, :].rearrange("p (w f) -> p w f", w=2)
            return whole[:, 0, :], whole[:, 1, :]

        @block.sync
        def _(sp):
            def load_chunk(c):
                raw, masks = stage(c % XS)
                if c >= XS:
                    sp.wait_ge(mw_lo_ready, c - XS + 1)
                cols = slice(c * CH * T, (c + 1) * CH * T)
                sp.dma_start(raw, weight_dram[:, cols]).then_inc(slot_moved[c % XS], 16)
                for g in range(G):
                    sp.dma_start(masks[g * R:(g + 1) * R, :], mask_dram[:, cols]).then_inc(slot_moved[c % XS], 16)

            def load_pair(i, slot):
                sp.dma_start(x_ring[:, slot, :].rearrange("p (b f) -> p b f", b=2),
                             x_dram[i]).then_inc(x_loaded[slot], 16)

            sp.dma_start(cond_rows[:], cond).then_inc(cond_loaded, 16)
            load_chunk(0)
            load_chunk(1)
            load_pair(0, 0)
            load_chunk(2)
            load_pair(1, 1)
            sp.dma_start(bias_rows[:], bias.rearrange("(a o) -> a o", a=1).broadcast_to([P, O])).then_inc(bias_loaded, 16)
            load_chunk(3)
            for c in range(XS, CHUNKS):
                load_chunk(c)
            load_pair(2, 2)
            load_pair(3, 3)

            def finish_pair(r, s, more):
                i = r * XS + s
                sp.wait_ge(evacuated, GEN + i + 1)
                sp.dma_start(out_dram[i], out_ring[:, s, :].rearrange("p (b f) -> p b f", b=2)).then_inc(slot_moved[s], 16)
                if more:
                    load_pair(i + XS, s)

            with sp.Fori(0, PAIRS // XS - 1) as r:
                for s in range(XS):
                    finish_pair(r, s, True)
            for s in range(XS):
                finish_pair(PAIRS // XS - 1, s, False)
            for s in range(XS):
                sp.wait_ge(slot_moved[s], LOADS + 16 * (PAIRS // XS))

        @block.gpsimd
        def _(pool):
            nc.gpsimd.memset(ident[:], 0.0).then_inc(ident_zeroed, 1)
            pool.wait_ge(ident_zeroed, 1)
            nc.gpsimd.affine_select(out=ident[:], in_=ident[:], compare_op=ALU.not_equal, fill=1.0, base=0,
                                    pattern=[[-1, P]], channel_multiplier=1).then_inc(ident_ready, 1)

            def mask_chunk(c):
                raw, masks = stage(c % XS)
                pool.wait_ge(slot_moved[c % XS], 16 * (1 + G) * (c // XS + 1))
                nc.gpsimd.tensor_tensor(raw, raw, masks, ALU.mult).then_inc(masked, 1)

            def low_chunk(c):
                raw, _ = stage(c % XS)
                pool.wait_ge(mw_hi_ready, c + 1)
                if c >= 2:
                    pool.wait_ge(products_ready, KC * (c - 1))
                nc.gpsimd.tensor_tensor(mw_lo[:, c % 2].rearrange("p q t -> p (q t)"), raw,
                                        mw_hi[:, c % 2].rearrange("p q t -> p (q t)").bitcast(F32),
                                        ALU.subtract).then_inc(mw_lo_ready, 1)

            mask_chunk(0)
            for c in range(CHUNKS):
                if c + 1 < CHUNKS:
                    mask_chunk(c + 1)
                low_chunk(c)

            pool.wait_ge(bias_loaded, 16)

            def add_bias(r, s):
                pool.wait_ge(transposed, r * XS + s + 1)
                rows = x_ring[:, s, :].rearrange("p (a o) -> p a o", o=O)
                nc.gpsimd.tensor_tensor(rows, rows, bias_rows[:].unsqueeze(1).broadcast_to([P, 2 * J, O]),
                                        ALU.add).then_inc(x_biased, 1)

            with pool.Fori(0, PAIRS // XS) as r:
                for s in range(XS):
                    add_bias(r, s)

        @block.tensor
        def _(pe):
            def transpose_pair(i, s, landed):
                pe.wait_ge(x_loaded[s % XS], landed)
                if not isinstance(i, int) or i >= 2:
                    pe.wait_ge(xt_lo_ready, i - 1)
                for k in range(KC):
                    for b in range(2):
                        for j in range(J):
                            src = x_ring[:, s % XS, :].rearrange("p (b j t) -> p b j t", b=2, j=J)
                            dst = transposes[:, s % 2, :].rearrange("p (k b j n) -> p k b j n", k=KC, b=2, j=J)
                            last = nc.tensor.transpose(dst[:, k, b, j, :], src[:, b, j, k * P:(k + 1) * P], ident[:])
                last.then_inc(transposed, 1)

            def weigh_chunk(c):
                pe.wait_ge(mw_hi_ready, c + 1)
                pe.wait_ge(mw_lo_ready, c + 1)
                for k in range(KC):
                    if c >= 1:
                        pe.wait_ge(evacuated, KC * (c - 1) + k + 1)
                    for q in range(CH):
                        high = mw_hi[:, c % 2, q, k * P:(k + 1) * P]
                        low = mw_lo[:, c % 2, q, k * P:(k + 1) * P]
                        dst = products[:, k, q * BANK:(q + 1) * BANK]
                        ym, yl = (y[:].rearrange("p b r -> p (b r)") for y in (y_hi, y_lo))
                        nc.tensor.matmul(dst, high, ym, start=True, stop=False)
                        nc.tensor.matmul(dst, high, yl, start=False, stop=False)
                        last = nc.tensor.matmul(dst, low, ym, start=False, stop=True)
                    last.then_inc(products_ready, 1)

            def multiply_pair(i, s):
                pe.wait_ge(xt_lo_ready, i + 1)
                pe.wait_ge(evacuated, GEN + i - 1)
                for b in range(2):
                    for j in range(J):
                        dst = products[:, s % 2, (b * J + j) * O:(b * J + j + 1) * O]
                        for k in range(KC):
                            high, low = xt_hi[:, s, k, b, j, :], xt_lo[:, s, k, b, j, :]
                            wh, wl = (w[:, k, 2 * i + b].rearrange("p q r -> p (q r)") for w in (w_hi, w_lo))
                            nc.tensor.matmul(dst, high, wh, start=(k == 0), stop=False)
                            nc.tensor.matmul(dst, high, wl, start=False, stop=False)
                            last = nc.tensor.matmul(dst, low, wh, start=False, stop=(k == KC - 1))
                last.then_inc(products_ready, 1)

            pe.wait_ge(ident_ready, 1)
            pe.wait_ge(cond_widened, 1)
            nc.tensor.transpose(transposes[:, 1, 0:B], cond_wide[:].rearrange("b g r -> b (g r)"),
                                ident[0:B, 0:B]).then_inc(yt_ready, 1)
            pe.wait_ge(y_ready, 2)
            weigh_chunk(0)
            weigh_chunk(1)
            transpose_pair(0, 0, 16)
            weigh_chunk(2)
            transpose_pair(1, 1, 16)
            for c in range(3, CHUNKS):
                weigh_chunk(c)

            pe.wait_ge(evacuated, GEN)
            with pe.Fori(0, PAIRS // XS - 1) as r:
                for s in range(XS):
                    i = r * XS + s
                    transpose_pair(i + 2, s + 2, 16 * (r + (s + 2) // XS + 1))
                    multiply_pair(i, s)
            r = PAIRS // XS - 1
            for s in range(XS):
                i = r * XS + s
                if i + 2 < PAIRS:
                    transpose_pair(i + 2, s + 2, 16 * (r + 1))
                multiply_pair(i, s)

        @block.scalar
        def _(act):
            act.wait_ge(yt_ready, 1)
            nc.scalar.copy(yt_hi[:], transposes[:, 1, 0:B]).then_inc(yt_hi_ready, 1)

            def high_chunk(c):
                raw, _ = stage(c % XS)
                act.wait_ge(masked, c + 1)
                if c >= 2:
                    act.wait_ge(products_ready, KC * (c - 1))
                nc.scalar.copy(mw_hi[:, c % 2].rearrange("p q t -> p (q t)"), raw).then_inc(mw_hi_ready, 1)

            def high_weights(c):
                for k in range(KC):
                    act.wait_ge(products_ready, KC * c + k + 1)
                    nc.scalar.copy(w_hi[:, k, :, CH * c:CH * (c + 1), :].rearrange("p b q r -> p q b r"),
                                   products[:, k, :].rearrange("p (q b r) -> p q b r", q=CH, r=R)
                                   ).then_inc(w_hi_ready, 1)

            def high_pair(i, s):
                act.wait_ge(transposed, i + 1)
                if not isinstance(i, int) or i >= XS:
                    act.wait_ge(products_ready, GEN + i - XS + 1)
                nc.scalar.copy(xt_hi[:, s % XS].rearrange("p k b j n -> p (k b j n)"),
                               transposes[:, s % 2, :]).then_inc(xt_hi_ready, 1)

            high_chunk(0)
            high_chunk(1)
            for c in range(CHUNKS):
                high_weights(c)
                if c + 2 < CHUNKS:
                    high_chunk(c + 2)
                if c in (1, 2):
                    high_pair(c - 1, c - 1)

            with act.Fori(0, PAIRS // XS - 1) as r:
                for s in range(XS):
                    high_pair(r * XS + s + 2, s + 2)
            r = PAIRS // XS - 1
            for s in range(XS - 2):
                high_pair(r * XS + s + 2, s + 2)

        @block.vector
        def _(dve):
            dve.wait_ge(cond_loaded, 16)
            nc.vector.tensor_copy(cond_wide[:], cond_rows[:].unsqueeze(2).broadcast_to([B, G, R])).then_inc(cond_widened, 1)
            dve.wait_ge(ident_ready, 1)
            nc.vector.tensor_reduce(diag[:], ident[:].rearrange("p (g r) -> p r g", r=R), axis=AX_X,
                                    op=ALU.add).then_inc(y_parts_ready, 1)
            dve.wait_ge(yt_hi_ready, 1)
            nc.vector.tensor_tensor(yt_lo[:], transposes[:, 1, 0:B], yt_hi[:].bitcast(F32),
                                    ALU.subtract).then_inc(y_parts_ready, 1)
            dve.wait_ge(y_parts_ready, 2)
            for y, yt in ((y_hi, yt_hi[:].bitcast(F32)), (y_lo, yt_lo[:])):
                nc.vector.tensor_tensor(y[:], yt.unsqueeze(2).broadcast_to([P, B, R]),
                                        diag[:].unsqueeze(1).broadcast_to([P, B, R]), ALU.mult).then_inc(y_ready, 1)

            def low_weights(c):
                for k in range(KC):
                    dve.wait_ge(w_hi_ready, KC * c + k + 1)
                    high, low = (w[:, k, :, CH * c:CH * (c + 1), :].rearrange("p b q r -> p q b r") for w in (w_hi, w_lo))
                    nc.vector.tensor_tensor(low, products[:, k, :].rearrange("p (q b r) -> p q b r", q=CH, r=R),
                                            high.bitcast(F32), ALU.subtract).then_inc(evacuated, 1)

            def low_pair(i, s):
                dve.wait_ge(xt_hi_ready, i + 1)
                high, low = (xt[:, s % XS].rearrange("p k b j n -> p (k b j n)") for xt in (xt_hi, xt_lo))
                nc.vector.tensor_tensor(low, transposes[:, s % 2, :], high.bitcast(F32),
                                        ALU.subtract).then_inc(xt_lo_ready, 1)

            def finish_pair(r, s):
                i = r * XS + s
                dve.wait_ge(products_ready, GEN + i + 1)
                dve.wait_ge(x_biased, i + 1)
                dve.wait_ge(slot_moved[s], LOADS + 16 * r)
                split = {"a": 2 * J, "r": R}
                nc.vector.tensor_tensor(
                    out_ring[:, s, :].rearrange("p (a r q) -> p a r q", **split),
                    products[:, s % 2, :].rearrange("p (a q r) -> p a r q", **split),
                    x_ring[:, s, :].rearrange("p (a r q) -> p a r q", **split), ALU.add).then_inc(evacuated, 1)

            for c in range(CHUNKS):
                low_weights(c)
                if c in (1, 2):
                    low_pair(c - 1, c - 1)

            with dve.Fori(0, PAIRS // XS - 1) as r:
                for s in range(XS):
                    low_pair(r * XS + s + 2, s + 2)
                    finish_pair(r, s)
            r = PAIRS // XS - 1
            for s in range(XS):
                if s + 2 < XS:
                    low_pair(r * XS + s + 2, s + 2)
                finish_pair(r, s)


_INS = ["x", "cond_8", "L0_cond_weight", "L0_cond_mask", "L0_cond_bias"]


def kernel(**inputs):
    import numpy as np
    import concourse.bacc as bacc
    from concourse.bass_utils import run_bass_kernel_spmd

    nc = bacc.Bacc("TRN2", target_bir_lowering=False, num_devices=1)
    arrays, args = {}, []
    for name in _INS:
        a = np.ascontiguousarray(inputs[name])
        arrays[f"in_{name}"] = a
        args.append(nc.dram_tensor(f"in_{name}", a.shape, mybir.dt.from_np(a.dtype), kind="ExternalInput").ap())
    shape = inputs["x"].shape
    out = nc.dram_tensor("out", shape, F32, kind="ExternalOutput").ap()
    conditional_residual(nc, *args, out)
    result = run_bass_kernel_spmd(nc, [arrays], core_ids=[0])
    return result.results[0]["out"]
```

```python
from contextlib import ExitStack

import concourse.bass as bass
from concourse import mybir

P = 128
F32 = mybir.dt.float32
F32R = mybir.dt.float32r
ALU = mybir.AluOpType
ACT = mybir.ActivationFunctionType
AX_X = mybir.AxisListType.X

BANK = 512
XS = 4
AHEAD = 3
CH = 2


def conditional_residual(nc, x, cond, weight, mask, bias, out):
    B, N, T = x.shape
    G, O, _ = weight.shape
    R = P // G
    Q = O // R
    KC = T // P
    J = N // P
    PAIRS = B // 2
    CHUNKS = Q // CH
    GEN = CHUNKS * KC
    LOADS = 16 * 2 * (CHUNKS // XS)
    PAIR = 2 * J * T
    assert O == N == T and B * R == BANK and CH * BANK == PAIR == KC * BANK and J * O == BANK
    assert PAIRS % XS == 0 and CHUNKS % XS == 0

    x_dram = x.rearrange("(i b) (p j) t -> i p b (j t)", b=2, j=J)
    out_dram = out.rearrange("(i b) (p j) o -> i p b (j o)", b=2, j=J)
    weight_dram = weight.rearrange("g (r q) t -> r g (q t)", q=Q)
    mask_dram = mask.rearrange("(r q) t -> r (q t)", q=Q)

    with ExitStack() as ctx:
        def sb(name, shape, dt=F32):
            return ctx.enter_context(nc.sbuf_tensor(name, shape, dt))

        def psum(name, shape):
            return ctx.enter_context(nc.psum_tensor(name, shape, F32))

        def sem(name):
            return ctx.enter_context(nc.semaphore(name))

        w_hi = sb("w_hi", [P, KC, B, Q, R], F32R)
        w_lo = sb("w_lo", [P, KC, B, Q, R], F32R)
        mw_hi = sb("mw_hi", [P, 2, CH, T], F32R)
        mw_lo = sb("mw_lo", [P, 2, CH, T], F32R)
        y_hi = sb("y_hi", [P, B, R], F32R)
        y_lo = sb("y_lo", [P, B, R], F32R)
        x_ring = sb("x_ring", [P, XS, PAIR])
        out_ring = sb("out_ring", [P, XS, PAIR])
        xt_hi = sb("xt_hi", [P, XS, KC, 2, J, P], F32R)
        xt_lo = sb("xt_lo", [P, XS, KC, 2, J, P], F32R)
        bias_rows = sb("bias_rows", [P, O])
        ident = sb("ident", [P, P])
        cond_rows = sb("cond_rows", [B, G])
        cond_wide = sb("cond_wide", [B, R, G])
        diag = sb("diag", [P, R])
        yt_hi = sb("yt_hi", [P, B], F32R)
        yt_lo = sb("yt_lo", [P, B])

        slots = psum("slots", [P, 4, PAIR])

        def transposes(pair):
            return slots[:, 2 * (pair % 2), :]

        def products(pair):
            return slots[:, 2 * (pair % 2) + 1, :]

        def weighed(c, k):
            return slots[:, 2 * k + (c + 1) % 2, :]

        yt_psum = weighed(0, 1)[:, 0:B]

        cond_loaded = sem("cond_loaded")
        bias_loaded = sem("bias_loaded")
        ident_zeroed = sem("ident_zeroed")
        ident_ready = sem("ident_ready")
        cond_widened = sem("cond_widened")
        yt_ready = sem("yt_ready")
        yt_hi_ready = sem("yt_hi_ready")
        y_parts_ready = sem("y_parts_ready")
        y_ready = sem("y_ready")
        slot_moved = [sem(f"slot_moved{s}") for s in range(XS)]
        masked = sem("masked")
        mw_hi_ready = sem("mw_hi_ready")
        mw_lo_ready = sem("mw_lo_ready")
        x_loaded = [sem(f"x_loaded{s}") for s in range(XS)]
        transposed = sem("transposed")
        xt_hi_ready = sem("xt_hi_ready")
        xt_lo_ready = sem("xt_lo_ready")
        x_biased = sem("x_biased")
        products_ready = sem("products_ready")
        w_hi_ready = sem("w_hi_ready")
        evacuated = sem("evacuated")

        block = ctx.enter_context(nc.Block())

        def stage(slot):
            whole = out_ring[:, slot, :].rearrange("p (w f) -> p w f", w=2)
            return whole[:, 0, :], whole[:, 1, :]

        def mask_chunk(engine, queue, c):
            raw, masks = stage(c % XS)
            queue.wait_ge(slot_moved[c % XS], 16 * 2 * (c // XS + 1))
            engine.tensor_tensor(raw, raw, masks, ALU.mult).then_inc(masked, 1)

        def low_chunk(engine, queue, c):
            raw, _ = stage(c % XS)
            queue.wait_ge(mw_hi_ready, c + 1)
            if c >= 2:
                queue.wait_ge(products_ready, KC * (c - 1))
            engine.tensor_tensor(mw_lo[:, c % 2].rearrange("p q t -> p (q t)"), raw,
                                 mw_hi[:, c % 2].rearrange("p q t -> p (q t)").bitcast(F32),
                                 ALU.subtract).then_inc(mw_lo_ready, 1)

        @block.sync
        def _(sp):
            def load_chunk(c):
                raw, masks = stage(c % XS)
                if c >= XS:
                    sp.wait_ge(mw_lo_ready, c - XS + 1)
                cols = slice(c * CH * T, (c + 1) * CH * T)
                sp.dma_start(raw, weight_dram[:, :, cols]).then_inc(slot_moved[c % XS], 16)
                sp.dma_start(masks, mask_dram[:, cols].unsqueeze(1).broadcast_to([R, G, CH * T])
                             ).then_inc(slot_moved[c % XS], 16)

            def load_pair(i, slot):
                sp.dma_start(x_ring[:, slot, :].rearrange("p (b f) -> p b f", b=2),
                             x_dram[i]).then_inc(x_loaded[slot], 16)

            sp.dma_start(cond_rows[:], cond).then_inc(cond_loaded, 16)
            load_chunk(0)
            load_pair(0, 0)
            load_chunk(1)
            load_pair(1, 1)
            load_chunk(2)
            sp.dma_start(bias_rows[:], bias.rearrange("(a o) -> a o", a=1).broadcast_to([P, O])).then_inc(bias_loaded, 16)
            load_chunk(3)
            for c in range(XS, CHUNKS):
                load_chunk(c)
            load_pair(2, 2)
            load_pair(3, 3)

            def store_pair(i, s):
                sp.wait_ge(evacuated, GEN + i + 1)
                sp.dma_start(out_dram[i], out_ring[:, s, :].rearrange("p (b f) -> p b f", b=2)).then_inc(slot_moved[s], 16)

            with sp.Fori(0, PAIRS // XS - 1) as r:
                for s in range(XS):
                    i = r * XS + s
                    sp.wait_ge(x_biased, i + 1)
                    load_pair(i + XS, s)
                    store_pair(i, s)
            for s in range(XS):
                store_pair(PAIRS - XS + s, s)
            for s in range(XS):
                sp.wait_ge(slot_moved[s], LOADS + 16 * (PAIRS // XS))

        @block.gpsimd
        def _(pool):
            nc.gpsimd.memset(ident[:], 0.0).then_inc(ident_zeroed, 1)
            pool.wait_ge(ident_zeroed, 1)
            nc.gpsimd.affine_select(out=ident[:], in_=ident[:], compare_op=ALU.not_equal, fill=1.0, base=0,
                                    pattern=[[-1, P]], channel_multiplier=1).then_inc(ident_ready, 1)

            pool.wait_ge(masked, 1)
            mask_chunk(nc.gpsimd, pool, 1)
            pool.wait_ge(mw_lo_ready, 1)
            for c in range(1, CHUNKS):
                if c + 1 < CHUNKS:
                    mask_chunk(nc.gpsimd, pool, c + 1)
                low_chunk(nc.gpsimd, pool, c)

            pool.wait_ge(bias_loaded, 16)

            def add_bias(r, s):
                pool.wait_ge(transposed, r * XS + s + 1)
                pool.wait_ge(slot_moved[s], LOADS + 16 * r)
                rows, biased = (ring[:, s, :].rearrange("p (a o) -> p a o", o=O) for ring in (x_ring, out_ring))
                nc.gpsimd.tensor_tensor(biased, rows, bias_rows[:].unsqueeze(1).broadcast_to([P, 2 * J, O]),
                                        ALU.add).then_inc(x_biased, 1)

            with pool.Fori(0, PAIRS // XS) as r:
                for s in range(XS):
                    add_bias(r, s)

        @block.tensor
        def _(pe):
            def transpose_pair(i, s, landed, later=True):
                pe.wait_ge(x_loaded[s % XS], landed)
                if later:
                    pe.wait_ge(xt_lo_ready, i - 1)
                for k in range(KC):
                    for b in range(2):
                        for j in range(J):
                            src = x_ring[:, s % XS, :].rearrange("p (b j t) -> p b j t", b=2, j=J)
                            dst = transposes(s).rearrange("p (k b j n) -> p k b j n", k=KC, b=2, j=J)
                            last = nc.tensor.transpose(dst[:, k, b, j, :], src[:, b, j, k * P:(k + 1) * P], ident[:])
                last.then_inc(transposed, 1)

            def weigh_chunk(c):
                pe.wait_ge(mw_hi_ready, c + 1)
                pe.wait_ge(mw_lo_ready, c + 1)
                for k in range(KC):
                    if c == 1:
                        pe.wait_ge(xt_lo_ready, k + 1)
                    if c >= 2:
                        pe.wait_ge(evacuated, KC * (c - 2) + k + 1)
                    for q in range(CH):
                        high = mw_hi[:, c % 2, q, k * P:(k + 1) * P]
                        low = mw_lo[:, c % 2, q, k * P:(k + 1) * P]
                        dst = weighed(c, k)[:, q * BANK:(q + 1) * BANK]
                        ym, yl = (y[:].rearrange("p b r -> p (b r)") for y in (y_hi, y_lo))
                        nc.tensor.matmul(dst, high, ym, start=True, stop=False)
                        nc.tensor.matmul(dst, high, yl, start=False, stop=False)
                        last = nc.tensor.matmul(dst, low, ym, start=False, stop=True)
                    last.then_inc(products_ready, 1)

            def multiply_pair(i, s):
                pe.wait_ge(xt_lo_ready, i + 1)
                pe.wait_ge(evacuated, GEN + i - 1)
                for b in range(2):
                    for j in range(J):
                        dst = products(s)[:, (b * J + j) * O:(b * J + j + 1) * O]
                        for k in range(KC):
                            high, low = xt_hi[:, s, k, b, j, :], xt_lo[:, s, k, b, j, :]
                            wh, wl = (w[:, k, 2 * i + b].rearrange("p q r -> p (q r)") for w in (w_hi, w_lo))
                            nc.tensor.matmul(dst, high, wh, start=(k == 0), stop=False)
                            nc.tensor.matmul(dst, high, wl, start=False, stop=False)
                            last = nc.tensor.matmul(dst, low, wh, start=False, stop=(k == KC - 1))
                last.then_inc(products_ready, 1)

            pe.wait_ge(ident_ready, 1)
            pe.wait_ge(cond_widened, 1)
            nc.tensor.transpose(yt_psum, cond_wide[:].rearrange("b r g -> b (r g)"),
                                ident[0:B, 0:B]).then_inc(yt_ready, 1)
            pe.wait_ge(y_ready, 2)
            transpose_pair(0, 0, 16, later=False)
            weigh_chunk(0)
            transpose_pair(1, 1, 16, later=False)
            for c in range(1, CHUNKS):
                weigh_chunk(c)
            pe.wait_ge(evacuated, GEN - 1)
            transpose_pair(2, 2, 16)
            pe.wait_ge(evacuated, GEN)
            with pe.Fori(0, PAIRS // XS - 1) as r:
                for s in range(XS):
                    i = r * XS + s
                    multiply_pair(i, s)
                    transpose_pair(i + AHEAD, s + AHEAD, 16 * (r + (s + AHEAD) // XS + 1))
            r = PAIRS // XS - 1
            for s in range(XS):
                i = r * XS + s
                multiply_pair(i, s)
                if i + AHEAD < PAIRS:
                    transpose_pair(i + AHEAD, s + AHEAD, 16 * (r + 1))

        @block.scalar
        def _(act):
            act.wait_ge(yt_ready, 1)
            nc.scalar.copy(yt_hi[:], yt_psum).then_inc(yt_hi_ready, 1)

            def high_chunk(c):
                raw, _ = stage(c % XS)
                act.wait_ge(masked, c + 1)
                if c >= 2:
                    act.wait_ge(products_ready, KC * (c - 1))
                nc.scalar.copy(mw_hi[:, c % 2].rearrange("p q t -> p (q t)"), raw).then_inc(mw_hi_ready, 1)

            def high_weights(c):
                for k in range(KC):
                    act.wait_ge(products_ready, KC * c + k + 1)
                    nc.scalar.copy(w_hi[:, k, :, CH * c:CH * (c + 1), :].rearrange("p b q r -> p q b r"),
                                   weighed(c, k).rearrange("p (q b r) -> p q b r", q=CH, r=R)
                                   ).then_inc(w_hi_ready, 1)

            def high_pair(i, s):
                act.wait_ge(transposed, i + 1)
                if not isinstance(i, int) or i >= XS:
                    act.wait_ge(products_ready, GEN + i - XS + 1)
                nc.scalar.copy(xt_hi[:, s % XS].rearrange("p k b j n -> p (k b j n)"),
                               transposes(s)).then_inc(xt_hi_ready, 1)

            high_chunk(0)
            high_pair(0, 0)
            high_chunk(1)
            for c in range(CHUNKS):
                high_weights(c)
                if c == 0:
                    high_pair(1, 1)
                if c + 2 < CHUNKS:
                    high_chunk(c + 2)
            high_pair(2, 2)

            with act.Fori(0, PAIRS // XS - 1) as r:
                for s in range(XS):
                    high_pair(r * XS + s + AHEAD, s + AHEAD)
            for i in range(PAIRS - XS + AHEAD, PAIRS):
                high_pair(i, i % XS)

        @block.vector
        def _(dve):
            dve.wait_ge(cond_loaded, 16)
            nc.vector.tensor_copy(cond_wide[:], cond_rows[:].unsqueeze(1).broadcast_to([B, R, G])).then_inc(cond_widened, 1)
            dve.wait_ge(ident_ready, 1)
            nc.vector.tensor_reduce(diag[:], ident[:].rearrange("p (r g) -> p r g", r=R), axis=AX_X,
                                    op=ALU.add).then_inc(y_parts_ready, 1)
            dve.wait_ge(yt_hi_ready, 1)
            nc.vector.tensor_tensor(yt_lo[:], yt_psum, yt_hi[:].bitcast(F32),
                                    ALU.subtract).then_inc(y_parts_ready, 1)
            dve.wait_ge(y_parts_ready, 2)
            for y, yt in ((y_hi, yt_hi[:].bitcast(F32)), (y_lo, yt_lo[:])):
                nc.vector.tensor_tensor(y[:], yt.unsqueeze(2).broadcast_to([P, B, R]),
                                        diag[:].unsqueeze(1).broadcast_to([P, B, R]), ALU.mult).then_inc(y_ready, 1)

            mask_chunk(nc.vector, dve, 0)
            low_chunk(nc.vector, dve, 0)

            def low_weights(c):
                for k in range(KC):
                    dve.wait_ge(w_hi_ready, KC * c + k + 1)
                    high, low = (w[:, k, :, CH * c:CH * (c + 1), :].rearrange("p b q r -> p q b r") for w in (w_hi, w_lo))
                    nc.vector.tensor_tensor(low, weighed(c, k).rearrange("p (q b r) -> p q b r", q=CH, r=R),
                                            high.bitcast(F32), ALU.subtract).then_inc(evacuated, 1)

            def low_pair(i, s):
                dve.wait_ge(xt_hi_ready, i + 1)
                high, low = (xt[:, s % XS].rearrange("p k b j n -> p (k b j n)") for xt in (xt_hi, xt_lo))
                nc.vector.tensor_tensor(low, transposes(s), high.bitcast(F32),
                                        ALU.subtract).then_inc(xt_lo_ready, 1)

            def finish_pair(r, s):
                i = r * XS + s
                dve.wait_ge(products_ready, GEN + i + 1)
                dve.wait_ge(x_biased, i + 1)
                result = out_ring[:, s, :].rearrange("p (a r q) -> p a r q", r=R, q=Q)
                nc.vector.tensor_tensor(result, products(s).rearrange("p (a q r) -> p a r q", r=R, q=Q),
                                        result, ALU.add).then_inc(evacuated, 1)

            low_pair(0, 0)
            for c in range(CHUNKS):
                low_weights(c)
                if c == 0:
                    low_pair(1, 1)
            low_pair(2, 2)

            with dve.Fori(0, PAIRS // XS - 1) as r:
                for s in range(XS):
                    finish_pair(r, s)
                    low_pair(r * XS + s + AHEAD, s + AHEAD)
            for s in range(XS):
                i = PAIRS - XS + s
                finish_pair(i // XS, s)
                if i + AHEAD < PAIRS:
                    low_pair(i + AHEAD, s + AHEAD)


_INS = ["x", "cond_8", "L0_cond_weight", "L0_cond_mask", "L0_cond_bias"]


def kernel(**inputs):
    import numpy as np
    import concourse.bacc as bacc
    from concourse.bass_utils import run_bass_kernel_spmd

    nc = bacc.Bacc("TRN2", target_bir_lowering=False, num_devices=1)
    arrays, args = {}, []
    for name in _INS:
        a = np.ascontiguousarray(inputs[name])
        arrays[f"in_{name}"] = a
        args.append(nc.dram_tensor(f"in_{name}", a.shape, mybir.dt.from_np(a.dtype), kind="ExternalInput").ap())
    shape = inputs["x"].shape
    out = nc.dram_tensor("out", shape, F32, kind="ExternalOutput").ap()
    conditional_residual(nc, *args, out)
    result = run_bass_kernel_spmd(nc, [arrays], core_ids=[0])
    return result.results[0]["out"]
```

```python
from contextlib import ExitStack

import concourse.bass as bass
from concourse import mybir

P = 128
F32 = mybir.dt.float32
F32R = mybir.dt.float32r
ALU = mybir.AluOpType
ACT = mybir.ActivationFunctionType
AX_X = mybir.AxisListType.X

BANK = 512
XS = 4
AHEAD = 3
WARM = 7
CH = 2


def conditional_residual(nc, x, cond, weight, mask, bias, out):
    B, N, T = x.shape
    G, O, _ = weight.shape
    R = P // G
    Q = O // R
    KC = T // P
    J = N // P
    PAIRS = B // 2
    CHUNKS = Q // CH
    GEN = CHUNKS * KC
    LOADS = 16 * 2 * (CHUNKS // XS)
    PAIR = 2 * J * T
    assert O == N == T and B * R == BANK and CH * BANK == PAIR == KC * BANK and J * O == BANK
    assert PAIRS % XS == 0 and CHUNKS % XS == 0

    x_dram = x.rearrange("(i b) (p j) t -> i p b (j t)", b=2, j=J)
    out_dram = out.rearrange("(i b) (p j) o -> i p b (j o)", b=2, j=J)
    weight_dram = weight.rearrange("g (r q) t -> r g (q t)", q=Q)
    mask_dram = mask.rearrange("(r q) t -> r (q t)", q=Q)

    with ExitStack() as ctx:
        def sb(name, shape, dt=F32):
            return ctx.enter_context(nc.sbuf_tensor(name, shape, dt))

        def psum(name, shape):
            return ctx.enter_context(nc.psum_tensor(name, shape, F32))

        def sem(name):
            return ctx.enter_context(nc.semaphore(name))

        w_hi = sb("w_hi", [P, KC, B, Q, R], F32R)
        w_lo = sb("w_lo", [P, KC, B, Q, R], F32R)
        mw_hi = sb("mw_hi", [P, 2, CH, T], F32R)
        mw_lo = sb("mw_lo", [P, 2, CH, T], F32R)
        y_hi = sb("y_hi", [P, B, R], F32R)
        y_lo = sb("y_lo", [P, B, R], F32R)
        x_ring = sb("x_ring", [P, XS, PAIR])
        out_ring = sb("out_ring", [P, XS, PAIR])
        xt_hi = sb("xt_hi", [P, XS, KC, 2, J, P], F32R)
        xt_lo = sb("xt_lo", [P, XS, KC, 2, J, P], F32R)
        bias_rows = sb("bias_rows", [P, O])
        ident = sb("ident", [P, P])
        cond_rows = sb("cond_rows", [B, G])
        cond_wide = sb("cond_wide", [B, R, G])
        diag = sb("diag", [P, R])
        yt_hi = sb("yt_hi", [P, B], F32R)
        yt_lo = sb("yt_lo", [P, B])

        slots = psum("slots", [P, 4, PAIR])

        def transposes(pair):
            return slots[:, 2 * (pair % 2) + 1, :]

        first_transposes = slots[:, 2, :]

        def products(pair):
            return slots[:, 2 * (pair % 2), :]

        def weighed(c, k):
            return slots[:, 2 * k + (c + 1) % 2, :]

        yt_psum = weighed(0, 1)[:, 0:B]

        cond_loaded = sem("cond_loaded")
        bias_loaded = sem("bias_loaded")
        ident_zeroed = sem("ident_zeroed")
        ident_ready = sem("ident_ready")
        cond_widened = sem("cond_widened")
        yt_ready = sem("yt_ready")
        yt_hi_ready = sem("yt_hi_ready")
        y_parts_ready = sem("y_parts_ready")
        y_ready = sem("y_ready")
        slot_moved = [sem(f"slot_moved{s}") for s in range(XS)]
        masked = sem("masked")
        mw_hi_ready = sem("mw_hi_ready")
        mw_lo_ready = sem("mw_lo_ready")
        x_loaded = [sem(f"x_loaded{s}") for s in range(XS)]
        transposed = sem("transposed")
        xt_hi_ready = sem("xt_hi_ready")
        xt_lo_ready = sem("xt_lo_ready")
        x_biased = sem("x_biased")
        products_ready = sem("products_ready")
        half_ready = sem("half_ready")
        half_done = sem("half_done")
        w_hi_ready = sem("w_hi_ready")
        evacuated = sem("evacuated")

        block = ctx.enter_context(nc.Block())

        def stage(slot):
            whole = out_ring[:, slot, :].rearrange("p (w f) -> p w f", w=2)
            return whole[:, 0, :], whole[:, 1, :]

        def mask_chunk(engine, queue, c):
            raw, masks = stage(c % XS)
            queue.wait_ge(slot_moved[c % XS], 16 * 2 * (c // XS + 1))
            engine.tensor_tensor(raw, raw, masks, ALU.mult).then_inc(masked, 1)

        def low_chunk(engine, queue, c):
            raw, _ = stage(c % XS)
            queue.wait_ge(mw_hi_ready, c + 1)
            if c >= 2:
                queue.wait_ge(products_ready, KC * (c - 1))
            engine.tensor_tensor(mw_lo[:, c % 2].rearrange("p q t -> p (q t)"), raw,
                                 mw_hi[:, c % 2].rearrange("p q t -> p (q t)").bitcast(F32),
                                 ALU.subtract).then_inc(mw_lo_ready, 1)

        @block.sync
        def _(sp):
            def load_chunk(c):
                raw, masks = stage(c % XS)
                if c >= XS:
                    sp.wait_ge(mw_lo_ready, c - XS + 1)
                cols = slice(c * CH * T, (c + 1) * CH * T)
                sp.dma_start(raw, weight_dram[:, :, cols]).then_inc(slot_moved[c % XS], 16)
                sp.dma_start(masks, mask_dram[:, cols].unsqueeze(1).broadcast_to([R, G, CH * T])
                             ).then_inc(slot_moved[c % XS], 16)

            def load_pair(i, slot):
                sp.dma_start(x_ring[:, slot, :].rearrange("p (b f) -> p b f", b=2),
                             x_dram[i]).then_inc(x_loaded[slot], 16)

            sp.dma_start(cond_rows[:], cond).then_inc(cond_loaded, 16)
            load_chunk(0)
            load_pair(0, 0)
            for c in range(1, CHUNKS):
                load_chunk(c)
            sp.dma_start(bias_rows[:], bias.rearrange("(a o) -> a o", a=1).broadcast_to([P, O])).then_inc(bias_loaded, 16)
            for i in range(1, XS):
                load_pair(i, i)

            with sp.Fori(0, PAIRS // XS - 1) as r:
                for s in range(XS):
                    sp.wait_ge(x_biased, r * XS + s + 1)
                    load_pair((r + 1) * XS + s, s)
            for s in range(XS):
                sp.wait_ge(slot_moved[s], LOADS + 16 * (PAIRS // XS + (s == XS - 1)))

        @block.gpsimd
        def _(pool):
            nc.gpsimd.memset(ident[:], 0.0).then_inc(ident_zeroed, 1)
            pool.wait_ge(ident_zeroed, 1)
            nc.gpsimd.affine_select(out=ident[:], in_=ident[:], compare_op=ALU.not_equal, fill=1.0, base=0,
                                    pattern=[[-1, P]], channel_multiplier=1).then_inc(ident_ready, 1)

            pool.wait_ge(masked, 2)
            mask_chunk(nc.gpsimd, pool, 2)
            pool.wait_ge(mw_lo_ready, 2)
            low_chunk(nc.gpsimd, pool, 2)
            mask_chunk(nc.gpsimd, pool, 3)
            mask_chunk(nc.gpsimd, pool, 4)
            mask_chunk(nc.gpsimd, pool, 5)
            pool.wait_ge(mw_lo_ready, 4)
            for c in range(4, CHUNKS):
                low_chunk(nc.gpsimd, pool, c)
                if c + 2 < CHUNKS:
                    mask_chunk(nc.gpsimd, pool, c + 2)

            pool.wait_ge(bias_loaded, 16)

            def add_bias(r, s):
                pool.wait_ge(transposed, r * XS + s + 1)
                pool.wait_ge(slot_moved[s], LOADS + 16 * r)
                rows, biased = (ring[:, s, :].rearrange("p (a o) -> p a o", o=O) for ring in (x_ring, out_ring))
                nc.gpsimd.tensor_tensor(biased, rows, bias_rows[:].unsqueeze(1).broadcast_to([P, 2 * J, O]),
                                        ALU.add).then_inc(x_biased, 1)

            with pool.Fori(0, PAIRS // XS) as r:
                for s in range(XS):
                    add_bias(r, s)

        @block.tensor
        def _(pe):
            def transpose_pair(s, whole, landed):
                pe.wait_ge(x_loaded[s], landed)
                for k in range(KC):
                    for b in range(2):
                        for j in range(J):
                            src = x_ring[:, s, :].rearrange("p (b j t) -> p b j t", b=2, j=J)
                            dst = whole.rearrange("p (k b j n) -> p k b j n", k=KC, b=2, j=J)
                            last = nc.tensor.transpose(dst[:, k, b, j, :], src[:, b, j, k * P:(k + 1) * P], ident[:])
                last.then_inc(transposed, 1)

            def weigh_chunk(c):
                pe.wait_ge(mw_hi_ready, c + 1)
                pe.wait_ge(mw_lo_ready, c + 1)
                for k in range(KC):
                    if c == 1 and k == 1:
                        pe.wait_ge(xt_lo_ready, 1)
                    if c >= 2:
                        pe.wait_ge(evacuated, KC * (c - 2) + k + 1)
                    for q in range(CH):
                        high = mw_hi[:, c % 2, q, k * P:(k + 1) * P]
                        low = mw_lo[:, c % 2, q, k * P:(k + 1) * P]
                        dst = weighed(c, k)[:, q * BANK:(q + 1) * BANK]
                        ym, yl = (y[:].rearrange("p b r -> p (b r)") for y in (y_hi, y_lo))
                        nc.tensor.matmul(dst, high, ym, start=True, stop=False)
                        nc.tensor.matmul(dst, high, yl, start=False, stop=False)
                        last = nc.tensor.matmul(dst, low, ym, start=False, stop=True)
                    last.then_inc(products_ready, 1)

            def multiply_pair(i, s):
                pe.wait_ge(xt_lo_ready, i + 1)
                pe.wait_ge(evacuated, GEN + i - 1)
                for b in range(2):
                    for j in range(J):
                        dst = products(s)[:, (b * J + j) * O:(b * J + j + 1) * O]
                        for k in range(KC):
                            high, low = xt_hi[:, s, k, b, j, :], xt_lo[:, s, k, b, j, :]
                            wh, wl = (w[:, k, 2 * i + b].rearrange("p q r -> p (q r)") for w in (w_hi, w_lo))
                            nc.tensor.matmul(dst, high, wh, start=(k == 0), stop=False)
                            nc.tensor.matmul(dst, high, wl, start=False, stop=False)
                            last = nc.tensor.matmul(dst, low, wh, start=False, stop=(k == KC - 1))
                    if b == 0 and isinstance(i, int) and i == PAIRS - 1:
                        last.then_inc(half_ready, 1)
                last.then_inc(products_ready, 1)

            pe.wait_ge(ident_ready, 1)
            pe.wait_ge(cond_widened, 1)
            nc.tensor.transpose(yt_psum, cond_wide[:].rearrange("b r g -> b (r g)"),
                                ident[0:B, 0:B]).then_inc(yt_ready, 1)
            for _ in range(WARM):
                nc.tensor.matmul(weighed(0, 0)[:, 0:P], ident[:], ident[:], start=True, stop=True)
            pe.wait_ge(y_ready, 2)
            transpose_pair(0, first_transposes, 16)
            for c in range(CHUNKS):
                weigh_chunk(c)
            for i in range(1, AHEAD):
                pe.wait_ge(evacuated, KC * (CHUNKS - 2) + i % 2 + 1)
                transpose_pair(i, transposes(i), 16)
            pe.wait_ge(evacuated, GEN)
            with pe.Fori(0, PAIRS // XS - 1) as r:
                for s in range(XS):
                    i = r * XS + s
                    multiply_pair(i, s)
                    pe.wait_ge(xt_lo_ready, i + AHEAD - 1)
                    transpose_pair((s + AHEAD) % XS, transposes(s + AHEAD), 16 * (r + (s + AHEAD) // XS + 1))
            for i in range(PAIRS - XS, PAIRS):
                multiply_pair(i, i % XS)
                if i + AHEAD < PAIRS:
                    pe.wait_ge(xt_lo_ready, i + AHEAD - 1)
                    transpose_pair((i + AHEAD) % XS, transposes(i + AHEAD), 16 * ((i + AHEAD) // XS + 1))

        @block.scalar
        def _(act):
            act.wait_ge(yt_ready, 1)
            nc.scalar.copy(yt_hi[:], yt_psum).then_inc(yt_hi_ready, 1)

            def high_chunk(c):
                raw, _ = stage(c % XS)
                act.wait_ge(masked, c + 1)
                if c >= 2:
                    act.wait_ge(products_ready, KC * (c - 1))
                nc.scalar.copy(mw_hi[:, c % 2].rearrange("p q t -> p (q t)"), raw).then_inc(mw_hi_ready, 1)

            def high_weights(c):
                for k in range(KC):
                    if k == 1 and c + 2 < CHUNKS:
                        high_chunk(c + 2)
                    act.wait_ge(products_ready, KC * c + k + 1)
                    nc.scalar.copy(w_hi[:, k, :, CH * c:CH * (c + 1), :].rearrange("p b q r -> p q b r"),
                                   weighed(c, k).rearrange("p (q b r) -> p q b r", q=CH, r=R)
                                   ).then_inc(w_hi_ready, 1)

            def high_pair(i, s, whole):
                act.wait_ge(transposed, i + 1)
                nc.scalar.copy(xt_hi[:, s].rearrange("p k b j n -> p (k b j n)"), whole).then_inc(xt_hi_ready, 1)

            def store_pair(i, s):
                act.wait_ge(evacuated, GEN + i + 1)
                act.dma_start(out_dram[i], out_ring[:, s, :].rearrange("p (b f) -> p b f", b=2)).then_inc(slot_moved[s], 16)

            high_chunk(0)
            high_pair(0, 0, first_transposes)
            high_chunk(1)
            for c in range(CHUNKS):
                high_weights(c)
            for i in range(1, AHEAD):
                high_pair(i, i, transposes(i))

            with act.Fori(0, PAIRS // XS - 1) as r:
                for s in range(XS):
                    i = r * XS + s
                    act.wait_ge(products_ready, GEN + i + AHEAD - XS + 1)
                    high_pair(i + AHEAD, (s + AHEAD) % XS, transposes(s + AHEAD))
                    store_pair(i, s)
            for i in range(PAIRS - XS, PAIRS - 1):
                if i + AHEAD < PAIRS:
                    act.wait_ge(products_ready, GEN + i + AHEAD - XS + 1)
                    high_pair(i + AHEAD, (i + AHEAD) % XS, transposes(i + AHEAD))
                store_pair(i, i % XS)
            for b, (done, count) in enumerate(((half_done, 1), (evacuated, GEN + PAIRS))):
                act.wait_ge(done, count)
                act.dma_start(out_dram[PAIRS - 1, :, b, :], out_ring[:, XS - 1, b * J * O:(b + 1) * J * O]
                              ).then_inc(slot_moved[XS - 1], 16)

        @block.vector
        def _(dve):
            dve.wait_ge(cond_loaded, 16)
            nc.vector.tensor_copy(cond_wide[:], cond_rows[:].unsqueeze(1).broadcast_to([B, R, G])).then_inc(cond_widened, 1)
            dve.wait_ge(ident_ready, 1)
            nc.vector.tensor_reduce(diag[:], ident[:].rearrange("p (r g) -> p r g", r=R), axis=AX_X,
                                    op=ALU.add).then_inc(y_parts_ready, 1)
            dve.wait_ge(yt_hi_ready, 1)
            nc.vector.tensor_tensor(yt_lo[:], yt_psum, yt_hi[:].bitcast(F32),
                                    ALU.subtract).then_inc(y_parts_ready, 1)
            dve.wait_ge(y_parts_ready, 2)
            for y, yt in ((y_hi, yt_hi[:].bitcast(F32)), (y_lo, yt_lo[:])):
                nc.vector.tensor_tensor(y[:], yt.unsqueeze(2).broadcast_to([P, B, R]),
                                        diag[:].unsqueeze(1).broadcast_to([P, B, R]), ALU.mult).then_inc(y_ready, 1)

            mask_chunk(nc.vector, dve, 0)
            low_chunk(nc.vector, dve, 0)
            mask_chunk(nc.vector, dve, 1)

            def low_weights(c):
                for k in range(KC):
                    if (c, k) == (1, 1):
                        dve.wait_ge(mw_lo_ready, 3)
                        low_chunk(nc.vector, dve, 3)
                    dve.wait_ge(w_hi_ready, KC * c + k + 1)
                    high, low = (w[:, k, :, CH * c:CH * (c + 1), :].rearrange("p b q r -> p q b r") for w in (w_hi, w_lo))
                    nc.vector.tensor_tensor(low, weighed(c, k).rearrange("p (q b r) -> p q b r", q=CH, r=R),
                                            high.bitcast(F32), ALU.subtract).then_inc(evacuated, 1)

            def low_pair(i, s, whole):
                dve.wait_ge(xt_hi_ready, i + 1)
                high, low = (xt[:, s].rearrange("p k b j n -> p (k b j n)") for xt in (xt_hi, xt_lo))
                nc.vector.tensor_tensor(low, whole, high.bitcast(F32),
                                        ALU.subtract).then_inc(xt_lo_ready, 1)

            def finish(s, batches, done):
                cols = slice(batches.start * J * O, batches.stop * J * O)
                result = out_ring[:, s, cols].rearrange("p (a r q) -> p a r q", r=R, q=Q)
                nc.vector.tensor_tensor(result, products(s)[:, cols].rearrange("p (a q r) -> p a r q", r=R, q=Q),
                                        result, ALU.add).then_inc(done, 1)

            def finish_pair(i, s):
                dve.wait_ge(products_ready, GEN + i + 1)
                dve.wait_ge(x_biased, i + 1)
                finish(s, range(0, 2), evacuated)

            low_chunk(nc.vector, dve, 1)
            low_pair(0, 0, first_transposes)
            for c in range(CHUNKS):
                low_weights(c)
            for i in range(1, AHEAD):
                low_pair(i, i, transposes(i))

            with dve.Fori(0, PAIRS // XS - 1) as r:
                for s in range(XS):
                    i = r * XS + s
                    finish_pair(i, s)
                    low_pair(i + AHEAD, (s + AHEAD) % XS, transposes(s + AHEAD))
            for i in range(PAIRS - XS, PAIRS - 1):
                finish_pair(i, i % XS)
                if i + AHEAD < PAIRS:
                    low_pair(i + AHEAD, (i + AHEAD) % XS, transposes(i + AHEAD))
            dve.wait_ge(x_biased, PAIRS)
            dve.wait_ge(half_ready, 1)
            finish(XS - 1, range(0, 1), half_done)
            dve.wait_ge(products_ready, GEN + PAIRS)
            finish(XS - 1, range(1, 2), evacuated)


_INS = ["x", "cond_8", "L0_cond_weight", "L0_cond_mask", "L0_cond_bias"]


def kernel(**inputs):
    import numpy as np
    import concourse.bacc as bacc
    from concourse.bass_utils import run_bass_kernel_spmd

    nc = bacc.Bacc("TRN2", target_bir_lowering=False, num_devices=1)
    arrays, args = {}, []
    for name in _INS:
        a = np.ascontiguousarray(inputs[name])
        arrays[f"in_{name}"] = a
        args.append(nc.dram_tensor(f"in_{name}", a.shape, mybir.dt.from_np(a.dtype), kind="ExternalInput").ap())
    shape = inputs["x"].shape
    out = nc.dram_tensor("out", shape, F32, kind="ExternalOutput").ap()
    conditional_residual(nc, *args, out)
    result = run_bass_kernel_spmd(nc, [arrays], core_ids=[0])
    return result.results[0]["out"]
```
